# Optimizing a Trainium2 kernel written in Bass

```python
import numpy as np
import jax
import jax.numpy as jnp

def _softmax(x, axis=-1):
    return jax.nn.softmax(x, axis=axis)

def _gelu(x):
    return jax.nn.gelu(x, approximate=True)

def _silu(x):
    return jax.nn.silu(x)

def _sigmoid(x):
    return jax.nn.sigmoid(x)

def _layernorm(x, axis=-1, eps=1e-05):
    m = jnp.mean(x, axis=axis, keepdims=True)
    v = jnp.var(x, axis=axis, keepdims=True)
    return (x - m) / jnp.sqrt(v + eps)

def _scatter_add(tgt, idx, src, axis=0):
    return tgt.at[idx].add(src)

def _segment_sum(src, seg, n):
    return jax.ops.segment_sum(src, seg, n)
kernel_name = 'mk_dlrm_tower_d1_rec_r8_c0af91'

def setup_inputs(seed: int=0):
    np.random.seed(seed)
    _w = jnp.asarray

    def _rec_inputs():
        import jax
        import jax.numpy as jnp
        _tk = jax.random.key(seed)
        dense_ctx = jax.random.normal(jax.random.fold_in(_tk, 190), (1024, 16), jnp.float32)
        ids = jnp.stack([jax.random.randint(jax.random.fold_in(_tk, 200 + f), (1024,), 0, v, jnp.int32) for f, v in enumerate([1000, 12500, 1250, 12500, 12500, 125000, 1250, 1000, 1000, 1250, 12500, 1000, 125000, 1000, 12500, 1000, 12500, 12500, 12500, 1000, 125000, 1250, 12500, 12500, 125000, 1250, 12500, 12500, 125000, 125000, 12500, 1000, 1250, 1250, 12500, 12500, 12500, 1250, 12500])], axis=1)
        tbl_0 = 0.05 * jax.random.normal(jax.random.fold_in(_tk, 500 + 0), (1000, 16), jnp.float32)
        tbl_1 = 0.05 * jax.random.normal(jax.random.fold_in(_tk, 500 + 1), (12500, 16), jnp.float32)
        tbl_2 = 0.05 * jax.random.normal(jax.random.fold_in(_tk, 500 + 2), (1250, 16), jnp.float32)
        tbl_3 = 0.05 * jax.random.normal(jax.random.fold_in(_tk, 500 + 3), (12500, 16), jnp.float32)
        tbl_4 = 0.05 * jax.random.normal(jax.random.fold_in(_tk, 500 + 4), (12500, 16), jnp.float32)
        tbl_5 = 0.05 * jax.random.normal(jax.random.fold_in(_tk, 500 + 5), (125000, 16), jnp.float32)
        tbl_6 = 0.05 * jax.random.normal(jax.random.fold_in(_tk, 500 + 6), (1250, 16), jnp.float32)
        tbl_7 = 0.05 * jax.random.normal(jax.random.fold_in(_tk, 500 + 7), (1000, 16), jnp.float32)
        tbl_8 = 0.05 * jax.random.normal(jax.random.fold_in(_tk, 500 + 8), (1000, 16), jnp.float32)
        tbl_9 = 0.05 * jax.random.normal(jax.random.fold_in(_tk, 500 + 9), (1250, 16), jnp.float32)
        tbl_10 = 0.05 * jax.random.normal(jax.random.fold_in(_tk, 500 + 10), (12500, 16), jnp.float32)
        tbl_11 = 0.05 * jax.random.normal(jax.random.fold_in(_tk, 500 + 11), (1000, 16), jnp.float32)
        tbl_12 = 0.05 * jax.random.normal(jax.random.fold_in(_tk, 500 + 12), (125000, 16), jnp.float32)
        tbl_13 = 0.05 * jax.random.normal(jax.random.fold_in(_tk, 500 + 13), (1000, 16), jnp.float32)
        tbl_14 = 0.05 * jax.random.normal(jax.random.fold_in(_tk, 500 + 14), (12500, 16), jnp.float32)
        tbl_15 = 0.05 * jax.random.normal(jax.random.fold_in(_tk, 500 + 15), (1000, 16), jnp.float32)
        tbl_16 = 0.05 * jax.random.normal(jax.random.fold_in(_tk, 500 + 16), (12500, 16), jnp.float32)
        tbl_17 = 0.05 * jax.random.normal(jax.random.fold_in(_tk, 500 + 17), (12500, 16), jnp.float32)
        tbl_18 = 0.05 * jax.random.normal(jax.random.fold_in(_tk, 500 + 18), (12500, 16), jnp.float32)
        tbl_19 = 0.05 * jax.random.normal(jax.random.fold_in(_tk, 500 + 19), (1000, 16), jnp.float32)
        tbl_20 = 0.05 * jax.random.normal(jax.random.fold_in(_tk, 500 + 20), (125000, 16), jnp.float32)
        tbl_21 = 0.05 * jax.random.normal(jax.random.fold_in(_tk, 500 + 21), (1250, 16), jnp.float32)
        tbl_22 = 0.05 * jax.random.normal(jax.random.fold_in(_tk, 500 + 22), (12500, 16), jnp.float32)
        tbl_23 = 0.05 * jax.random.normal(jax.random.fold_in(_tk, 500 + 23), (12500, 16), jnp.float32)
        tbl_24 = 0.05 * jax.random.normal(jax.random.fold_in(_tk, 500 + 24), (125000, 16), jnp.float32)
        tbl_25 = 0.05 * jax.random.normal(jax.random.fold_in(_tk, 500 + 25), (1250, 16), jnp.float32)
        tbl_26 = 0.05 * jax.random.normal(jax.random.fold_in(_tk, 500 + 26), (12500, 16), jnp.float32)
        tbl_27 = 0.05 * jax.random.normal(jax.random.fold_in(_tk, 500 + 27), (12500, 16), jnp.float32)
        tbl_28 = 0.05 * jax.random.normal(jax.random.fold_in(_tk, 500 + 28), (125000, 16), jnp.float32)
        tbl_29 = 0.05 * jax.random.normal(jax.random.fold_in(_tk, 500 + 29), (125000, 16), jnp.float32)
        tbl_30 = 0.05 * jax.random.normal(jax.random.fold_in(_tk, 500 + 30), (12500, 16), jnp.float32)
        tbl_31 = 0.05 * jax.random.normal(jax.random.fold_in(_tk, 500 + 31), (1000, 16), jnp.float32)
        tbl_32 = 0.05 * jax.random.normal(jax.random.fold_in(_tk, 500 + 32), (1250, 16), jnp.float32)
        tbl_33 = 0.05 * jax.random.normal(jax.random.fold_in(_tk, 500 + 33), (1250, 16), jnp.float32)
        tbl_34 = 0.05 * jax.random.normal(jax.random.fold_in(_tk, 500 + 34), (12500, 16), jnp.float32)
        tbl_35 = 0.05 * jax.random.normal(jax.random.fold_in(_tk, 500 + 35), (12500, 16), jnp.float32)
        tbl_36 = 0.05 * jax.random.normal(jax.random.fold_in(_tk, 500 + 36), (12500, 16), jnp.float32)
        tbl_37 = 0.05 * jax.random.normal(jax.random.fold_in(_tk, 500 + 37), (1250, 16), jnp.float32)
        tbl_38 = 0.05 * jax.random.normal(jax.random.fold_in(_tk, 500 + 38), (12500, 16), jnp.float32)
        _rk = jax.random.fold_in(_tk, 7)
        W_top1 = 0.0606339 * jax.random.normal(jax.random.fold_in(_tk, 801), (272, 512), jnp.float32)
        W_top2 = 0.0441942 * jax.random.normal(jax.random.fold_in(_tk, 802), (512, 256), jnp.float32)
        W_top3 = 0.0625 * jax.random.normal(jax.random.fold_in(_tk, 803), (256, 1), jnp.float32)
        b_top1 = jnp.zeros((512,), jnp.float32)
        b_top2 = jnp.zeros((256,), jnp.float32)
        return (dense_ctx, ids, tbl_0, tbl_1, tbl_2, tbl_3, tbl_4, tbl_5, tbl_6, tbl_7, tbl_8, tbl_9, tbl_10, tbl_11, tbl_12, tbl_13, tbl_14, tbl_15, tbl_16, tbl_17, tbl_18, tbl_19, tbl_20, tbl_21, tbl_22, tbl_23, tbl_24, tbl_25, tbl_26, tbl_27, tbl_28, tbl_29, tbl_30, tbl_31, tbl_32, tbl_33, tbl_34, tbl_35, tbl_36, tbl_37, tbl_38, W_top1, b_top1, W_top2, b_top2, W_top3)
    dense_ctx, ids, tbl_0, tbl_1, tbl_2, tbl_3, tbl_4, tbl_5, tbl_6, tbl_7, tbl_8, tbl_9, tbl_10, tbl_11, tbl_12, tbl_13, tbl_14, tbl_15, tbl_16, tbl_17, tbl_18, tbl_19, tbl_20, tbl_21, tbl_22, tbl_23, tbl_24, tbl_25, tbl_26, tbl_27, tbl_28, tbl_29, tbl_30, tbl_31, tbl_32, tbl_33, tbl_34, tbl_35, tbl_36, tbl_37, tbl_38, W_top1, b_top1, W_top2, b_top2, W_top3 = _rec_inputs()

    def _L0_rec_setup():
        import jax, jax.numpy as jnp
        import numpy as np
        B, M, D = (1024, 39, 16)
        S1, S2 = (128, 128)

        def _cin_layer(x0, xk, W, b):
            out = jnp.einsum('bhd,bmd,shm->bsd', xk, x0, W) + b[None, :, None]
            return jax.nn.relu(out)
        key = jax.random.key(seed)
        k0, k1, k2 = jax.random.split(key, 3)
        x0 = jax.random.normal(k0, (B, M, D), dtype=jnp.float32)
        W1 = jax.random.normal(k1, (S1, M, M), dtype=jnp.float32) * 0.05
        b1 = jnp.zeros((S1,), dtype=jnp.float32)
        W2 = jax.random.normal(k2, (S2, S1, M), dtype=jnp.float32) * 0.05
        b2 = jnp.zeros((S2,), dtype=jnp.float32)
        return {'x0': x0, 'W1': W1, 'b1': b1, 'W2': W2, 'b2': b2}
    _L0_rec_all = _L0_rec_setup()
    _L0_rec_in = {k: v for k, v in _L0_rec_all.items() if k in ('W1', 'b1', 'W2', 'b2')}
    del _L0_rec_all
    return {'dense_ctx': dense_ctx, 'ids': ids, 'tbl_0': tbl_0, 'tbl_1': tbl_1, 'tbl_2': tbl_2, 'tbl_3': tbl_3, 'tbl_4': tbl_4, 'tbl_5': tbl_5, 'tbl_6': tbl_6, 'tbl_7': tbl_7, 'tbl_8': tbl_8, 'tbl_9': tbl_9, 'tbl_10': tbl_10, 'tbl_11': tbl_11, 'tbl_12': tbl_12, 'tbl_13': tbl_13, 'tbl_14': tbl_14, 'tbl_15': tbl_15, 'tbl_16': tbl_16, 'tbl_17': tbl_17, 'tbl_18': tbl_18, 'tbl_19': tbl_19, 'tbl_20': tbl_20, 'tbl_21': tbl_21, 'tbl_22': tbl_22, 'tbl_23': tbl_23, 'tbl_24': tbl_24, 'tbl_25': tbl_25, 'tbl_26': tbl_26, 'tbl_27': tbl_27, 'tbl_28': tbl_28, 'tbl_29': tbl_29, 'tbl_30': tbl_30, 'tbl_31': tbl_31, 'tbl_32': tbl_32, 'tbl_33': tbl_33, 'tbl_34': tbl_34, 'tbl_35': tbl_35, 'tbl_36': tbl_36, 'tbl_37': tbl_37, 'tbl_38': tbl_38, 'W_top1': W_top1, 'b_top1': b_top1, 'W_top2': W_top2, 'b_top2': b_top2, 'W_top3': W_top3, 'L0_rec_W1': _L0_rec_in['W1'], 'L0_rec_b1': _L0_rec_in['b1'], 'L0_rec_W2': _L0_rec_in['W2'], 'L0_rec_b2': _L0_rec_in['b2']}

def reference(dense_ctx, ids, tbl_0, tbl_1, tbl_2, tbl_3, tbl_4, tbl_5, tbl_6, tbl_7, tbl_8, tbl_9, tbl_10, tbl_11, tbl_12, tbl_13, tbl_14, tbl_15, tbl_16, tbl_17, tbl_18, tbl_19, tbl_20, tbl_21, tbl_22, tbl_23, tbl_24, tbl_25, tbl_26, tbl_27, tbl_28, tbl_29, tbl_30, tbl_31, tbl_32, tbl_33, tbl_34, tbl_35, tbl_36, tbl_37, tbl_38, W_top1, b_top1, W_top2, b_top2, W_top3, L0_rec_W1, L0_rec_b1, L0_rec_W2, L0_rec_b2):
    import jax
    import jax.numpy as jnp

    def _L0_rec_ref(x0, W1, b1, W2, b2):
        import jax, jax.numpy as jnp
        import numpy as np
        B, M, D = (1024, 39, 16)
        S1, S2 = (128, 128)

        def _cin_layer(x0, xk, W, b):
            out = jnp.einsum('bhd,bmd,shm->bsd', xk, x0, W) + b[None, :, None]
            return jax.nn.relu(out)
        x1 = _cin_layer(x0, x0, W1, b1)
        x2 = _cin_layer(x0, x1, W2, b2)
        p1 = x1.sum(axis=-1)
        p2 = x2.sum(axis=-1)
        return jnp.concatenate([p1, p2], axis=-1)
    e = jnp.stack([tbl_0[ids[:, 0]], tbl_1[ids[:, 1]], tbl_2[ids[:, 2]], tbl_3[ids[:, 3]], tbl_4[ids[:, 4]], tbl_5[ids[:, 5]], tbl_6[ids[:, 6]], tbl_7[ids[:, 7]], tbl_8[ids[:, 8]], tbl_9[ids[:, 9]], tbl_10[ids[:, 10]], tbl_11[ids[:, 11]], tbl_12[ids[:, 12]], tbl_13[ids[:, 13]], tbl_14[ids[:, 14]], tbl_15[ids[:, 15]], tbl_16[ids[:, 16]], tbl_17[ids[:, 17]], tbl_18[ids[:, 18]], tbl_19[ids[:, 19]], tbl_20[ids[:, 20]], tbl_21[ids[:, 21]], tbl_22[ids[:, 22]], tbl_23[ids[:, 23]], tbl_24[ids[:, 24]], tbl_25[ids[:, 25]], tbl_26[ids[:, 26]], tbl_27[ids[:, 27]], tbl_28[ids[:, 28]], tbl_29[ids[:, 29]], tbl_30[ids[:, 30]], tbl_31[ids[:, 31]], tbl_32[ids[:, 32]], tbl_33[ids[:, 33]], tbl_34[ids[:, 34]], tbl_35[ids[:, 35]], tbl_36[ids[:, 36]], tbl_37[ids[:, 37]], tbl_38[ids[:, 38]]], axis=1)
    z = _L0_rec_ref(e, L0_rec_W1, L0_rec_b1, L0_rec_W2, L0_rec_b2)
    z = z.reshape(z.shape[0], -1)
    h = jnp.concatenate([z, dense_ctx], axis=1)
    h = jnp.maximum(h @ W_top1 + b_top1, 0.0)
    h = jnp.maximum(h @ W_top2 + b_top2, 0.0)
    y = h @ W_top3
    return y

_drawn_inputs = setup_inputs


def setup_inputs(seed=0):
    import zlib

    import numpy as np

    out = dict(_drawn_inputs(seed))
    spreads = {'b_top1': (0.0, 0.1),
     'b_top2': (0.0, 0.1),
     'L0_rec_b1': (0.0, 0.1),
     'L0_rec_b2': (0.0, 0.1)}
    factors = {'tbl_0': 4.674,
     'tbl_1': 4.495,
     'tbl_2': 6.971,
     'tbl_3': 6.178,
     'tbl_4': 6.773,
     'tbl_5': 7.276,
     'tbl_6': 5.991,
     'tbl_7': 4.59,
     'tbl_8': 8.0,
     'tbl_9': 7.782,
     'tbl_10': 6.045,
     'tbl_11': 5.594,
     'tbl_12': 5.576,
     'tbl_14': 7.806,
     'tbl_15': 6.325,
     'tbl_16': 7.431,
     'tbl_17': 4.893,
     'tbl_18': 5.405,
     'tbl_19': 4.499,
     'tbl_20': 8.0,
     'tbl_21': 3.288,
     'tbl_22': 8.0,
     'tbl_23': 7.22,
     'tbl_24': 7.754,
     'tbl_25': 5.057,
     'tbl_26': 4.465,
     'tbl_27': 6.443,
     'tbl_28': 8.0,
     'tbl_29': 5.207,
     'tbl_30': 4.851,
     'tbl_31': 3.054,
     'tbl_32': 8.0,
     'tbl_33': 7.722,
     'tbl_34': 7.758,
     'tbl_35': 7.267,
     'tbl_36': 8.0,
     'tbl_37': 8.0,
     'tbl_38': 6.5,
     'tbl_13': 4.079}
    for name, (base, spread) in spreads.items():
        noise = np.random.default_rng([zlib.crc32(name.encode()), seed]).standard_normal(out[name].shape)
        drawn = base * np.exp(spread * noise) if base else spread * noise
        out[name] = jnp.asarray(drawn.astype(out[name].dtype))
    for name, factor in factors.items():
        out[name] = (out[name] * factor).astype(out[name].dtype)
    return out
```

```python
from contextlib import ExitStack

import numpy as np
import concourse.bass as bass
from concourse import mybir

F32 = mybir.dt.float32
F32R = mybir.dt.float32r
BF16 = mybir.dt.bfloat16
I32 = mybir.dt.int32
ALU = mybir.AluOpType
ACT = mybir.ActivationFunctionType
AX = mybir.AxisListType

P = 128
B, M, D = 1024, 39, 16
S = 128
NCTX, N1, N2 = 16, 512, 256
DC = 4
CH = DC * P
TILES = B // P
CPT = D // DC
CHUNKS = TILES * CPT
PARTS = 3
KP = 3
NF = 7
NK = M // 2 + 1
ML, HL = 4, 32
NG = S // HL
NJ = 10
NSPREAD = 1 + NF + NJ
F_ROWS = [M * min(KP, NK - KP * t) for t in range(NF)]
J_ROWS = [HL * min(ML, M - ML * j) for j in range(NJ)]

WHOLE, BY_DVE, BY_POOL = "whole", "dve", "pool"
F_MODE = [[WHOLE] * NF] * CPT
J_MODE = [[WHOLE] * NJ] * CPT

SEQ = [("T", 0), ("J", 0), ("A", 0), ("F", 0), ("J", 1), ("F", 1), ("J", 2), ("F", 2),
       ("J", 3), ("F", 3), ("J", 4), ("F", 4), ("J", 5), ("F", 5), ("J", 6), ("F", 6),
       ("X1", 0), ("J", 7), ("J", 8), ("J", 9), ("X2", 0)]
NS = len(SEQ)
MLP_AT = {7: 1, 11: 2, 15: 3}
SPREAD_AHEAD = 4
SUB_LAG = 2
X_LAG = 2
ACC_LAG = 3
GATHER_SHARE = {3: range(0, 11), 0: range(11, 22), 1: range(22, 33), 2: range(33, 39)}

PARTS_AT = 14

Z_RING, H_RING = 4, 2


def spread_matrices():
    sel = np.zeros((PARTS * M, NSPREAD, P), np.float32)
    for part in range(PARTS):
        for k in range(KP):
            for h in range(M):
                sel[part * M + h, 0, k * M + h] = 1.0
                for t in range(NF):
                    if KP * t + k < NK:
                        sel[part * M + (h + KP * t + k) % M, 1 + t, k * M + h] = 1.0
        for j in range(NJ):
            for m in range(ML):
                if ML * j + m < M:
                    sel[part * M + ML * j + m, 1 + NF + j, m * HL:(m + 1) * HL] = 1.0
    return sel


def pair_weights(w1):
    w1 = np.asarray(w1)
    ahead = np.zeros((P, NF, S), w1.dtype)
    back = np.zeros((P, NF, S), w1.dtype)
    for t in range(NF):
        for k in range(KP * t, min(KP * t + KP, NK)):
            for h in range(M):
                p = (k - KP * t) * M + h
                ahead[p, t] = w1[:, h, (h + k) % M]
                if k:
                    back[p, t] = w1[:, (h + k) % M, h]
    return ahead, back


def cross_weights(w2):
    w2 = np.asarray(w2)
    out = np.zeros((ML, HL, NJ, NG, S), w2.dtype)
    for j in range(NJ):
        for m in range(ML):
            if ML * j + m < M:
                out[m, :, j] = w2[:, :, ML * j + m].T.reshape(NG, HL, S).transpose(1, 0, 2)
    return out.reshape(P, NJ, NG, S)


def build(nc, dram, tables, out):
    f_split = any(m != WHOLE for row in F_MODE for m in row)
    j_split = any(m != WHOLE for row in J_MODE for m in row)

    with ExitStack() as ctx:
        def sb(name, shape, dt=F32):
            return ctx.enter_context(nc.sbuf_tensor(name, shape, dt))

        def ps(name, shape, dt=F32):
            return ctx.enter_context(nc.psum_tensor(name, shape, dt))

        def sem(name):
            return ctx.enter_context(nc.semaphore(name))

        w2 = sb("w2", [P, NJ, NG, S])
        w2h = sb("w2h", [P, NJ, NG, S], F32R) if j_split else None
        w2l = sb("w2l", [P, NJ, NG, S], F32R) if j_split else None
        w1 = sb("w1", [P, NF, S])
        w1h = sb("w1h", [P, NF, S], F32R) if f_split else None
        w1l = sb("w1l", [P, NF, S], F32R) if f_split else None
        spread = sb("spread", [P, NSPREAD, P], BF16)
        wt1 = sb("wt1", [P, 3, N1])
        wt2 = sb("wt2", [P, N1 // P, N2])
        wt3 = sb("wt3", [P, N2 // P])
        bias1 = sb("bias1", [P, 1])
        bias2 = sb("bias2", [P, 1])
        biast1 = sb("biast1", [P, N1 // P])
        biast2 = sb("biast2", [P, N2 // P])
        ident = sb("ident", [P, P], BF16)
        ctx_t = sb("ctx_t", [P, P])
        idx = sb("idx", [P, M], I32)
        emb = sb("emb", [P, M * D])
        rest = sb("rest", [P, M * D])
        embp = sb("embp", [P, PARTS, M * D], BF16)
        e_t = sb("e_t", [P, 2, CH], BF16)
        a_sb = sb("a_sb", [P, 2, CH])
        zf = sb("zf", [P, Z_RING, CH])
        zfh = sb("zfh", [P, H_RING, CH], F32R) if f_split else None
        zfl = sb("zfl", [P, H_RING, CH], F32R) if f_split else None
        zj = sb("zj", [P, Z_RING, NG, CH])
        zjh = sb("zjh", [P, H_RING, NG, CH], F32R) if j_split else None
        zjl = sb("zjl", [P, H_RING, NG, CH], F32R) if j_split else None
        x1 = sb("x1", [P, 2, CH])
        x1r = sb("x1r", [P, 2, NG, CH])
        x2 = sb("x2", [P, 2, CH])
        acc1 = sb("acc1", [P, CH])
        acc2 = sb("acc2", [P, CH])
        p1 = sb("p1", [P, P])
        p2 = sb("p2", [P, P])
        h1 = sb("h1", [P, N1 // P, P])
        h2 = sb("h2", [P, N2 // P, P])
        y = sb("y", [P, 1])

        w1_back = zj[:, 0, :, :].rearrange("p g n -> p (g n)")[:, 0:NF * S]
        spread_f = zj[:, 1:3, :, :].rearrange("p r g n -> p (r g n)")[0:PARTS * M, 0:NSPREAD * P]
        ident_f = x1[:, 0, 0:P]

        bank_f = ps("bank_f", [P, 2, CH])
        bank_j = ps("bank_j", [P, 2, CH])
        l1_acc = ps("l1_acc", [P, CH])
        l2_acc = ps("l2_acc", [P, 2, CH])
        misc = ps("misc", [P, CH])
        misc_t = misc[:, :].bitcast(BF16)

        in_w2, in_w1, in_small = sem("in_w2"), sem("in_w1"), sem("in_small")
        in_spread, in_ident = sem("in_spread"), sem("in_ident")
        in_idx, in_ctx, in_emb = sem("in_idx"), sem("in_ctx"), sem("in_emb")
        gather_begun, out_done = sem("gather_begun"), sem("out_done")
        spread_ready, w1_summed = sem("spread_ready"), sem("w1_summed")
        w_rounded, w_ready = sem("w_rounded"), sem("w_ready")
        parts_step, parts_done = sem("parts_step"), sem("parts_done")
        transposed, et_ready = sem("transposed"), sem("et_ready")
        f_spread, j_spread, a_copied = sem("f_spread"), sem("j_spread"), sem("a_copied")
        f_made, j_made = sem("f_made"), sem("j_made")
        f_rounded, j_rounded = sem("f_rounded"), sem("j_rounded")
        f_sub = {BY_DVE: sem("f_sub_dve"), BY_POOL: sem("f_sub_pool")}
        j_sub = {BY_DVE: sem("j_sub_dve"), BY_POOL: sem("j_sub_pool")}
        f_used, j_used = sem("f_used"), sem("j_used")
        x1_done, x2_done, x1_spread = sem("x1_done"), sem("x2_done"), sem("x1_spread")
        acc1_done, acc2_done = sem("acc1_done"), sem("acc2_done")
        p1_done, p2_done = sem("p1_done"), sem("p2_done")
        mlp_mm, mlp_act, y_free = sem("mlp_mm"), sem("mlp_act"), sem("y_free")

        def upto(i, q, per_chunk, t=0):
            return i * (CPT * per_chunk) + (q * per_chunk + t)

        def mlp_upto(tile, layer):
            return (tile + 1) * 3 + layer

        def split_upto(modes, kinds, i, q, t):
            n = len(modes[0])
            row = [m in kinds for r in modes for m in r]
            k = q * n + t
            while k < 0:
                i, k = i - 1, k + CPT * n
            while k > CPT * n:
                i, k = i + 1, k - CPT * n
            return i * sum(row) + sum(row[:k])

        def wait(eng, s, value):
            if isinstance(value, int) and value <= 0:
                return
            eng.wait_ge(s, value)

        class Work:

            def __init__(self, modes, made, rounded, sub, used, z, zh, zl):
                self.modes, self.n = modes, len(modes[0])
                self.made, self.rounded, self.sub, self.used = made, rounded, sub, used
                self.z, self.zh, self.zl = z, zh, zl

            def mode(self, q, t):
                k = (q * self.n + t) % (CPT * self.n)
                return self.modes[k // self.n][k % self.n]

            def slot(self, q, t, ring):
                return (q * self.n + t) % ring

            def z_free(self, eng, i, q, t):
                u = t - Z_RING
                mode = self.mode(q, u)
                if mode == WHOLE:
                    wait(eng, self.used, upto(i, q, self.n, u + 1))
                else:
                    wait(eng, self.rounded, split_upto(self.modes, (BY_DVE, BY_POOL), i, q, u + 1))
                    wait(eng, self.sub[mode], split_upto(self.modes, (mode,), i, q, u + 1))

            def part_free(self, eng, i, q, t):
                wait(eng, self.used, upto(i, q, self.n, t - H_RING + 1))

        F = Work(F_MODE, f_made, f_rounded, f_sub, f_used, zf, zfh, zfl)
        J = Work(J_MODE, j_made, j_rounded, j_sub, j_used, zj, zjh, zjl)

        def has(kind, c):
            if c is None:
                return True
            return 0 <= c < CHUNKS if kind in ("J", "X2") else 0 <= c + 1 < CHUNKS

        def item(i, q, c, k):
            dq = k // NS
            kind, t = SEQ[k % NS]
            if not has(kind, None if c is None else c + dq):
                return None
            q += dq
            return kind, t, i, q if kind in ("J", "X2") else q + 1

        LOOP_TILES = TILES - 2

        def run(eng, step):
            step(0, -1, -1)
            step(0, 0, 0)
            step(0, 1, 1)
            with eng.Fori(0, LOOP_TILES) as i:
                for q in range(2, CPT + 2):
                    step(i, q, None)
            for c in range(CPT * LOOP_TILES + 2, CHUNKS + 1):
                step(c // CPT, c % CPT, c)

        def norm(i, q):
            return i + q // CPT, q % CPT

        block = ctx.enter_context(nc.Block())

        @block.sync
        def _(sp):
            sp.sem_inc(mlp_mm, 3)
            sp.sem_inc(mlp_act, 3)
            sp.sem_inc(y_free, 1)
            sp.dma_start(idx[:, :], dram["ids"][0:P, :]).then_inc(in_idx, 16)
            sp.dma_start(spread_f, dram["spread"]).then_inc(in_spread, 16)
            sp.dma_start(ident_f, dram["ident"]).then_inc(in_ident, 16)
            sp.dma_start(w1[:, :, :], dram["w1_ahead"]).then_inc(in_w1, 16)
            sp.dma_start(w1_back, dram["w1_back"].rearrange("p t s -> p (t s)")).then_inc(in_w1, 16)
            sp.dma_start(w2[:, :, :, :], dram["w2"]).then_inc(in_w2, 16)
            sp.dma_start(wt1[:, 0:2, :], dram["W_top1"][0:2 * S, :].rearrange("(k p) n -> p k n", p=P)
                         ).then_inc(in_small, 16)
            sp.dma_start(wt1[0:NCTX, 2, :], dram["W_top1"][2 * S:, :]).then_inc(in_small, 16)
            sp.dma_start(wt2[:, :, :], dram["W_top2"].rearrange("(k p) n -> p k n", p=P)).then_inc(in_small, 16)
            for dst, name in ((wt3, "W_top3"), (bias1, "b1"), (bias2, "b2"), (biast1, "b_top1"),
                              (biast2, "b_top2")):
                sp.dma_start(dst[:, :], dram[name]).then_inc(in_small, 16)

            def step(i, q, c):
                tile, cq = norm(i, q)
                if cq == CPT - 1 and (c is None or tile + 2 < TILES):
                    rows = bass.ds((tile + 2) * P, P)
                    wait(sp, in_emb, (tile + 2) * (16 * M))
                    sp.dma_start(idx[:, :], dram["ids"][rows, :]).then_inc(in_idx, 16)
                if cq == 0 and (c is None or c > 0):
                    store(tile - 1)
                for k in range(NS):
                    it = item(i, q, c, k - X_LAG)
                    if it and it[0] == "X1":
                        spread_x1(it[2], it[3])

            def spread_x1(i, q):
                s = q % 2
                wait(sp, x1_done, upto(i, q, 1, 1))
                for r in range(ML):
                    for g in range(NG):
                        sp.dma_start(x1r[HL * r:HL * (r + 1), s, g, :], x1[HL * g:HL * (g + 1), s, :]
                                     ).then_inc(x1_spread, 16)

            def store(tile):
                row = tile * P
                sp.wait_ge(mlp_mm, mlp_upto(tile, 0))
                sp.dma_start(ctx_t[0:NCTX, :], dram["ctx_t"][:, bass.ds(row, P)]).then_inc(in_ctx, 16)
                sp.wait_ge(mlp_act, mlp_upto(tile, 3))
                sp.dma_start(out[bass.ds(row, P), :], y[:, :]).then_inc(out_done, 16)
                sp.wait_ge(out_done, (tile + 1) * 16)
                sp.sem_inc(y_free, 1)

            run(sp, step)
            sp.wait_ge(out_done, 16 * TILES)

        @block.gpsimd
        def _(pool):
            def gather(tile, fields):
                for f in fields:
                    if f == 0:
                        wait(pool, parts_done, tile)
                        pool.wait_ge(in_idx, (tile + 1) * 16)
                        pool.sem_inc(gather_begun, 1)
                    nc.gpsimd.indirect_dma_start(
                        out=emb[:, f * D:(f + 1) * D], out_offset=None, in_=tables[f],
                        in_offset=bass.IndirectOffsetOnAxis(ap=idx[:, f:f + 1], axis=0),
                    ).then_inc(in_emb, 16)

            def subtract(w, t, i, q):
                if w.mode(q, t) != BY_POOL:
                    return
                w.part_free(pool, i, q, t)
                pool.wait_ge(w.rounded, split_upto(w.modes, (BY_DVE, BY_POOL), i, q, t + 1))
                zs, hs = w.slot(q, t, Z_RING), w.slot(q, t, H_RING)
                nc.gpsimd.tensor_tensor(w.zl[:, hs], w.z[:, zs], w.zh[:, hs].bitcast(F32),
                                        ALU.subtract).then_inc(w.sub[BY_POOL], 1)

            def step(i, q, c):
                tile, cq = norm(i, q)
                tile += 2 if cq == CPT - 1 else 1
                fields = list(GATHER_SHARE[cq]) if c is None or tile < TILES else []
                for k in range(NS):
                    if fields and k % 2 == 0:
                        gather(tile, [fields.pop(0)])
                    it = item(i, q, c, k - SUB_LAG)
                    if it and it[0] in "FJ":
                        subtract(F if it[0] == "F" else J, it[1], it[2], it[3])

            gather(0, range(M))
            run(pool, step)

        @block.scalar
        def _(act):
            act.wait_ge(in_ident, 16)
            nc.scalar.copy(ident[:, :], ident_f).then_inc(spread_ready, 1)
            act.wait_ge(in_spread, 16)
            nc.scalar.copy(spread[0:PARTS * M, :, :].rearrange("p u n -> p (u n)"), spread_f
                           ).then_inc(spread_ready, 1)
            if f_split:
                act.wait_ge(w1_summed, 1)
                nc.scalar.copy(w1h[:, :, :], w1[:, :, :]).then_inc(w_rounded, 1)
            if j_split:
                act.wait_ge(in_w2, 16)
                nc.scalar.copy(w2h[:, :, :, :], w2[:, :, :, :]).then_inc(w_rounded, 1)
            act.wait_ge(in_small, 16 * 8)

            def copy_transposed(i, q):
                act.wait_ge(transposed, upto(i, q, 1, 1))
                wait(act, j_spread, upto(i, q - 1, NJ))
                nc.scalar.copy(e_t[0:PARTS * M, q % 2, :], misc_t[0:PARTS * M, 0:CH]).then_inc(et_ready, 1)

            def copy_a(i, q):
                act.wait_ge(f_spread, upto(i, q, 1 + NF, 1))
                wait(act, f_made, upto(i, q - 1, NF))
                nc.scalar.copy(a_sb[:, q % 2, :], bank_f[:, 0, :]).then_inc(a_copied, 1)

            def round_z(w, t, i, q):
                if w.mode(q, t) == WHOLE:
                    return
                w.part_free(act, i, q, t)
                act.wait_ge(w.made, upto(i, q, w.n, t + 1))
                nc.scalar.copy(w.zh[:, w.slot(q, t, H_RING)], w.z[:, w.slot(q, t, Z_RING)]
                               ).then_inc(w.rounded, 1)

            def end_layer1(i, q):
                act.wait_ge(f_used, upto(i, q, NF, NF))
                wait(act, x1_spread, upto(i, q - 1, 16 * ML * NG))
                wait(act, acc1_done, upto(i, q - 1, 1))
                wait(act, j_made, upto(i, q - 1, NJ))
                nc.scalar.activation(x1[:, q % 2, :], l1_acc[:, :], ACT.Relu, bias=bias1[:, 0:1]
                                     ).then_inc(x1_done, 1)

            def end_layer2(i, q):
                act.wait_ge(j_used, upto(i, q, NJ, NJ))
                wait(act, acc2_done, upto(i, q - 1, 1))
                nc.scalar.activation(x2[:, q % 2, :], l2_acc[:, q % 2, :], ACT.Relu, bias=bias2[:, 0:1]
                                     ).then_inc(x2_done, 1)

            def mlp(tile, layer):
                act.wait_ge(mlp_mm, mlp_upto(tile, layer))
                if layer == 3:
                    act.wait_ge(y_free, tile + 1)
                    nc.scalar.copy(y[:, :], misc[:, 0:1]).then_inc(mlp_act, 1)
                    return
                dst, bias, n = ((h1, biast1, N1), (h2, biast2, N2))[layer - 1]
                for k in range(n // P):
                    last = nc.scalar.activation(dst[:, k, :], misc[:, k * P:(k + 1) * P], ACT.Relu,
                                                bias=bias[:, k:k + 1])
                last.then_inc(mlp_act, 1)

            def step(i, q, c):
                tile, cq = norm(i, q)
                for k in range(NS):
                    it = item(i, q, c, k)
                    if it and it[0] == "T":
                        copy_transposed(it[2], it[3])
                    if it and it[0] == "A":
                        copy_a(it[2], it[3])
                    if it and it[0] in "FJ":
                        round_z(F if it[0] == "F" else J, it[1], it[2], it[3])
                    it = item(i, q, c, k - X_LAG)
                    if it and it[0] == "X1":
                        end_layer1(it[2], it[3])
                    if it and it[0] == "X2":
                        end_layer2(it[2], it[3])
                    if cq == 0 and (c is None or c > 0) and k in MLP_AT:
                        mlp(tile - 1, MLP_AT[k])

            run(act, step)

        @block.vector
        def _(dve):
            dve.wait_ge(in_w1, 32)
            nc.vector.tensor_tensor(w1[:, :, :].rearrange("p t s -> p (t s)"),
                                    w1[:, :, :].rearrange("p t s -> p (t s)"), w1_back,
                                    ALU.add).then_inc(w1_summed, 1)
            if f_split:
                dve.wait_ge(w1_summed, 1)
                dve.wait_ge(w_rounded, 1)
                nc.vector.tensor_tensor(w1l[:, :, :], w1[:, :, :], w1h[:, :, :].bitcast(F32),
                                        ALU.subtract).then_inc(w_ready, 1)
            if j_split:
                dve.wait_ge(w_rounded, 1 + f_split)
                nc.vector.tensor_tensor(w2l[:, :, :, :], w2[:, :, :, :], w2h[:, :, :, :].bitcast(F32),
                                        ALU.subtract).then_inc(w_ready, 1)
            dve.wait_ge(w1_summed, 1)
            dve.wait_ge(spread_ready, 2)

            def make_parts(tile):
                dve.wait_ge(in_emb, (tile + 1) * (16 * M))
                wait(dve, transposed, tile * CPT)
                nc.vector.tensor_copy(embp[:, 0, :], emb[:, :]).then_inc(parts_step, 1)
                dve.wait_ge(parts_step, tile * 3 + 1)
                nc.vector.tensor_tensor(rest[:, :], emb[:, :], embp[:, 0, :], ALU.subtract
                                        ).then_inc(parts_step, 1)
                dve.wait_ge(parts_step, tile * 3 + 2)
                nc.vector.tensor_copy(embp[:, 1, :], rest[:, :]).then_inc(parts_step, 1)
                dve.wait_ge(parts_step, tile * 3 + 3)
                nc.vector.tensor_tensor(embp[:, 2, :], rest[:, :], embp[:, 1, :], ALU.subtract
                                        ).then_inc(parts_done, 1)

            def make_f(t, i, q):
                dve.wait_ge(f_spread, upto(i, q, 1 + NF, t + 2))
                if t == 0:
                    dve.wait_ge(a_copied, upto(i, q, 1, 1))
                F.z_free(dve, i, q, t)
                nc.vector.tensor_tensor(zf[:, F.slot(q, t, Z_RING), :], a_sb[:, q % 2, :],
                                        bank_f[:, (t + 1) % 2, :], ALU.mult).then_inc(f_made, 1)

            def make_j(t, i, q):
                dve.wait_ge(j_spread, upto(i, q, NJ, t + 1))
                if t == 0:
                    dve.wait_ge(x1_spread, upto(i, q, 16 * ML * NG, 16 * ML * NG))
                J.z_free(dve, i, q, t)
                e_row = bank_j[:, t % 2:t % 2 + 1, :].broadcast_to([P, NG, CH])
                nc.vector.tensor_tensor(zj[:, J.slot(q, t, Z_RING)], x1r[:, q % 2], e_row,
                                        ALU.mult).then_inc(j_made, 1)

            def subtract(w, t, i, q):
                if w.mode(q, t) != BY_DVE:
                    return
                w.part_free(dve, i, q, t)
                dve.wait_ge(w.rounded, split_upto(w.modes, (BY_DVE, BY_POOL), i, q, t + 1))
                zs, hs = w.slot(q, t, Z_RING), w.slot(q, t, H_RING)
                nc.vector.tensor_tensor(w.zl[:, hs], w.z[:, zs], w.zh[:, hs].bitcast(F32),
                                        ALU.subtract).then_inc(w.sub[BY_DVE], 1)

            def sum_d(i, q, x, x_done, acc, acc_done, p, p_done):
                tile, cq = norm(i, q)
                dve.wait_ge(x_done, upto(i, q, 1, 1))
                if cq == 0:
                    wait(dve, p_done, tile)
                    nc.vector.tensor_copy(acc[:, :], x[:, q % 2, :]).then_inc(acc_done, 1)
                    return
                dve.wait_ge(acc_done, upto(i, q, 1))
                nc.vector.tensor_tensor(acc[:, :], acc[:, :], x[:, q % 2, :], ALU.add).then_inc(acc_done, 1)
                if cq == CPT - 1:
                    dve.wait_ge(acc_done, upto(i, q, 1, 1))
                    dve.wait_ge(mlp_mm, mlp_upto(tile, 0))
                    nc.vector.tensor_reduce(p[:, :], acc[:, :].rearrange("p (d b) -> p b d", d=DC),
                                            AX.X, ALU.add).then_inc(p_done, 1)

            def step(i, q, c):
                tile, cq = norm(i, q)
                if c == -1:
                    make_parts(0)
                for k in range(NS):
                    it = item(i, q, c, k)
                    if it and it[0] == "F":
                        make_f(it[1], it[2], it[3])
                    if it and it[0] == "J":
                        make_j(it[1], it[2], it[3])
                    it = item(i, q, c, k - SUB_LAG)
                    if it and it[0] in "FJ":
                        subtract(F if it[0] == "F" else J, it[1], it[2], it[3])
                    it = item(i, q, c, k - ACC_LAG)
                    if it and it[0] == "X1":
                        sum_d(it[2], it[3], x1, x1_done, acc1, acc1_done, p1, p1_done)
                    if it and it[0] == "X2":
                        sum_d(it[2], it[3], x2, x2_done, acc2, acc2_done, p2, p2_done)
                    if k == PARTS_AT and cq == 2 and (c is None or tile + 1 < TILES):
                        make_parts(tile + 1)

            run(dve, step)

        @block.tensor
        def _(pe):
            pe.wait_ge(spread_ready, 2)
            pe.wait_ge(w1_summed, 1)
            pe.wait_ge(in_w2, 16)
            wait(pe, w_ready, f_split + j_split)
            pe.wait_ge(in_small, 16 * 8)
            emb_by_d = embp[:, :, :].rearrange("p a (f d) -> p d (a f)", d=D)

            def transpose_chunk(i, q, c):
                tile, cq = norm(i, q)
                pe.wait_ge(parts_done, tile + 1)
                wait(pe, et_ready, upto(i, q, 1))
                if c is None or c > 0:
                    pe.wait_ge(mlp_act, mlp_upto(tile - (1 if cq < 2 else 0), 0))
                for d in range(DC):
                    last = nc.tensor.transpose(misc_t[0:PARTS * M, d * P:(d + 1) * P],
                                               emb_by_d[:, cq * DC + d, :], ident[:, :])
                last.then_inc(transposed, 1)

            def spread_f_rows(u, i, q):
                if u == 0:
                    pe.wait_ge(et_ready, upto(i, q, 1, 1))
                if u == 2:
                    pe.wait_ge(a_copied, upto(i, q, 1, 1))
                else:
                    wait(pe, f_made, upto(i, q, NF, u - 2 if u > 2 else u - 1))
                nc.tensor.matmul(bank_f[:, u % 2, :], spread[0:PARTS * M, u, :],
                                 e_t[0:PARTS * M, q % 2, :], start=True, stop=True).then_inc(f_spread, 1)

            def spread_j_rows(t, i, q):
                wait(pe, j_made, upto(i, q, NJ, t - 1))
                nc.tensor.matmul(bank_j[:, t % 2, :], spread[0:PARTS * M, 1 + NF + t, :],
                                 e_t[0:PARTS * M, q % 2, :], start=True, stop=True).then_inc(j_spread, 1)

            def contract(w, t, i, q, acc, rows, tiles):
                mode = w.mode(q, t)
                if mode == WHOLE:
                    pe.wait_ge(w.made, upto(i, q, w.n, t + 1))
                    passes = [(0, 3)]
                else:
                    pe.wait_ge(w.rounded, split_upto(w.modes, (BY_DVE, BY_POOL), i, q, t + 1))
                    passes = [(1, 4), (2, 4), (1, 5)]
                for k, (a, b) in enumerate(passes):
                    if b == 5:
                        pe.wait_ge(w.sub[mode], split_upto(w.modes, (mode,), i, q, t + 1))
                    for g, ops in enumerate(tiles):
                        last = nc.tensor.matmul(acc, ops[a][0:rows], ops[b][0:rows],
                                                start=(t == 0 and k == 0 and g == 0),
                                                stop=(t == w.n - 1 and k == len(passes) - 1
                                                      and g == len(tiles) - 1))
                last.then_inc(w.used, 1)

            def contract_f(t, i, q):
                if t == 0:
                    wait(pe, x1_done, upto(i, q, 1))
                zs, hs = F.slot(q, t, Z_RING), F.slot(q, t, H_RING)
                split = F.mode(q, t) != WHOLE
                contract(F, t, i, q, l1_acc[:, :], F_ROWS[t],
                         [(w1[:, t, :], split and w1h[:, t, :], split and w1l[:, t, :],
                           zf[:, zs, :], split and zfh[:, hs, :], split and zfl[:, hs, :])])

            def contract_j(t, i, q):
                if t == 0:
                    wait(pe, x2_done, upto(i, q - 1, 1))
                zs, hs = J.slot(q, t, Z_RING), J.slot(q, t, H_RING)
                split = J.mode(q, t) != WHOLE
                contract(J, t, i, q, l2_acc[:, q % 2, :], J_ROWS[t],
                         [(w2[:, t, g, :], split and w2h[:, t, g, :], split and w2l[:, t, g, :],
                           zj[:, zs, g, :], split and zjh[:, hs, g, :], split and zjl[:, hs, g, :])
                          for g in range(NG)])

            def mlp(tile, layer):
                if layer == 1:
                    pe.wait_ge(p1_done, tile + 1)
                    pe.wait_ge(p2_done, tile + 1)
                    pe.wait_ge(in_ctx, (tile + 1) * 16)
                    if isinstance(tile, int) and tile == TILES - 1:
                        pe.wait_ge(et_ready, CHUNKS)
                    else:
                        pe.wait_ge(et_ready, upto(tile + 1, 1, 1, 1))
                    src = [(p1[:, :], wt1[:, 0, :]), (p2[:, :], wt1[:, 1, :]),
                           (ctx_t[0:NCTX, :], wt1[0:NCTX, 2, :])]
                    n = N1
                elif layer == 2:
                    pe.wait_ge(mlp_act, mlp_upto(tile, 1))
                    src = [(h1[:, k, :], wt2[:, k, :]) for k in range(N1 // P)]
                    n = N2
                else:
                    pe.wait_ge(mlp_act, mlp_upto(tile, 2))
                    for k in range(N2 // P):
                        last = nc.tensor.matmul(misc[:, 0:1], h2[:, k, :], wt3[:, k:k + 1],
                                                start=(k == 0), stop=(k == N2 // P - 1))
                    last.then_inc(mlp_mm, 1)
                    return
                for o in range(n // P):
                    for k, (x, w) in enumerate(src):
                        last = nc.tensor.matmul(misc[:, o * P:(o + 1) * P], w[:, o * P:(o + 1) * P], x,
                                                start=(k == 0), stop=(k == len(src) - 1))
                last.then_inc(mlp_mm, 1)

            def spread_item(it, c):
                if it is None:
                    return
                if it[0] == "T":
                    transpose_chunk(it[2], it[3], c)
                if it[0] == "A":
                    spread_f_rows(0, it[2], it[3])
                if it[0] == "F":
                    spread_f_rows(it[1] + 1, it[2], it[3])
                if it[0] == "J":
                    spread_j_rows(it[1], it[2], it[3])

            def step(i, q, c):
                tile, cq = norm(i, q)
                if c == -1:
                    for k in range(SPREAD_AHEAD):
                        spread_item(item(i, q, c, k), c)
                for k in range(NS):
                    it = item(i, q, c, k)
                    spread_item(item(i, q, c, k + SPREAD_AHEAD), c)
                    if it and it[0] == "F":
                        contract_f(it[1], it[2], it[3])
                    if it and it[0] == "J":
                        contract_j(it[1], it[2], it[3])
                    if cq == 0 and (c is None or c > 0) and k in MLP_AT:
                        mlp(tile - 1, MLP_AT[k])

            run(pe, step)


def kernel(**inputs):
    from concourse import bacc
    from concourse.bass_utils import run_bass_kernel_spmd

    nc = bacc.Bacc("TRN2", target_bir_lowering=False, num_devices=1)
    arrays = {}

    def load(name, a):
        a = np.ascontiguousarray(a)
        arrays[name] = a
        return nc.dram_tensor(name, a.shape, mybir.dt.from_np(a.dtype), kind="ExternalInput").ap()

    def columns(a):
        return np.asarray(a).reshape(-1, P).T

    ahead, back = pair_weights(inputs["L0_rec_W1"])
    dram = {
        "ids": load("ids", inputs["ids"]),
        "spread": load("spread_const", spread_matrices().reshape(PARTS * M, NSPREAD * P)),
        "ident": load("ident_const", np.eye(P, dtype=np.float32)),
        "w1_ahead": load("w1_ahead", ahead),
        "w1_back": load("w1_back", back),
        "w2": load("w2_pairs", cross_weights(inputs["L0_rec_W2"])),
        "ctx_t": load("ctx_transposed", np.asarray(inputs["dense_ctx"]).T),
        "W_top1": load("w_top1", inputs["W_top1"]),
        "W_top2": load("w_top2", inputs["W_top2"]),
        "W_top3": load("w_top3", columns(inputs["W_top3"])),
        "b1": load("cin_b1", columns(inputs["L0_rec_b1"])),
        "b2": load("cin_b2", columns(inputs["L0_rec_b2"])),
        "b_top1": load("mlp_b1", columns(inputs["b_top1"])),
        "b_top2": load("mlp_b2", columns(inputs["b_top2"])),
    }
    tables = [load(f"tbl_{f}", inputs[f"tbl_{f}"]) for f in range(M)]
    out = nc.dram_tensor("y_out", (B, 1), F32, kind="ExternalOutput").ap()
    build(nc, dram, tables, out)
    result = run_bass_kernel_spmd(nc, [arrays], core_ids=[0])
    return result.results[0]["y_out"]
```

```python
from contextlib import ExitStack

import numpy as np
import concourse.bass as bass
from concourse import mybir

F32 = mybir.dt.float32
F32R = mybir.dt.float32r
BF16 = mybir.dt.bfloat16
I32 = mybir.dt.int32
ALU = mybir.AluOpType
ACT = mybir.ActivationFunctionType
AX = mybir.AxisListType

P = 128
B, M, D = 1024, 39, 16
S = 128
NCTX, N1, N2 = 16, 512, 256
DC = 4
CH = DC * P
TILES = B // P
CPT = D // DC
CHUNKS = TILES * CPT
PARTS = 3
KP = 3
NF = 7
NK = M // 2 + 1
ML, HL = 4, 32
NG = S // HL
NJ = 10
NSPREAD = 1 + NF + NJ
F_ROWS = [M * min(KP, NK - KP * t) for t in range(NF)]
J_ROWS = [HL * min(ML, M - ML * j) for j in range(NJ)]

WHOLE, BY_DVE, BY_POOL = "whole", "dve", "pool"
NH = 2
GH = NG // NH
NU = NJ * NH
F_MODE = [[BY_POOL, BY_DVE, BY_POOL, BY_DVE, BY_POOL, BY_DVE, BY_POOL]] * CPT
J_MODE = [[BY_POOL, BY_DVE, BY_POOL, BY_POOL, WHOLE, WHOLE, BY_POOL, BY_DVE, BY_POOL, BY_POOL] * 2] * CPT

SEQ = [("J", 0, 0), ("J", 1, 0), ("F", 3, 1), ("J", 2, 0), ("J", 3, 0), ("F", 4, 1), ("J", 4, 0),
       ("J", 5, 0), ("F", 5, 1), ("J", 6, 0), ("J", 7, 0), ("F", 6, 1), ("X1", 0, 1), ("J", 8, 0),
       ("J", 9, 0), ("J", 10, 0), ("J", 11, 0), ("J", 12, 0), ("T", 0, 2), ("J", 13, 0),
       ("J", 14, 0), ("A", 0, 2), ("J", 15, 0), ("F", 0, 2), ("J", 16, 0), ("J", 17, 0),
       ("F", 1, 2), ("J", 18, 0), ("J", 19, 0), ("X2", 0, 0), ("F", 2, 2)]
NS = len(SEQ)
MLP_AT = {2: 1, 5: 2, 8: 3}
SPREAD_AHEAD = 8
SUB_LAG = 3
X_LAG = 8
ACC_LAG = 9
GATHER_SHARE = {2: range(0, 8), 3: range(8, 19), 0: range(19, 30), 1: range(30, M)}
GATHER_AT = range(4, NS, 2)
PARTS_AT = 2

F_RING = (4, 4, 4)
J_RING = (8, 5, 5)
E_RING = 4


def spread_matrices():
    sel = np.zeros((PARTS * M, NSPREAD, P), np.float32)
    for part in range(PARTS):
        for k in range(KP):
            for h in range(M):
                sel[part * M + h, 0, k * M + h] = 1.0
                for t in range(NF):
                    if KP * t + k < NK:
                        sel[part * M + (h + KP * t + k) % M, 1 + t, k * M + h] = 1.0
        for j in range(NJ):
            for m in range(ML):
                if ML * j + m < M:
                    sel[part * M + ML * j + m, 1 + NF + j, m * HL:(m + 1) * HL] = 1.0
    return sel


def pair_weights(w1):
    w1 = np.asarray(w1)
    ahead = np.zeros((P, NF, S), w1.dtype)
    back = np.zeros((P, NF, S), w1.dtype)
    for t in range(NF):
        for k in range(KP * t, min(KP * t + KP, NK)):
            for h in range(M):
                p = (k - KP * t) * M + h
                ahead[p, t] = w1[:, h, (h + k) % M]
                if k:
                    back[p, t] = w1[:, (h + k) % M, h]
    return ahead, back


def cross_weights(w2):
    w2 = np.asarray(w2)
    out = np.zeros((ML, HL, NJ, NG, S), w2.dtype)
    for j in range(NJ):
        for m in range(ML):
            if ML * j + m < M:
                out[m, :, j] = w2[:, :, ML * j + m].T.reshape(NG, HL, S).transpose(1, 0, 2)
    return out.reshape(P, NJ, NG, S)


def build(nc, dram, tables, out):
    f_split = any(m != WHOLE for row in F_MODE for m in row)
    j_whole = [j for j in range(NJ) if any(m == WHOLE for row in J_MODE for m in row[NH * j:NH * (j + 1)])]
    j_split = [j for j in range(NJ) if any(m != WHOLE for row in J_MODE for m in row[NH * j:NH * (j + 1)])]

    with ExitStack() as ctx:
        def sb(name, shape, dt=F32):
            return ctx.enter_context(nc.sbuf_tensor(name, shape, dt))

        def ps(name, shape, dt=F32):
            return ctx.enter_context(nc.psum_tensor(name, shape, dt))

        def sem(name):
            return ctx.enter_context(nc.semaphore(name))

        w2 = sb("w2", [P, len(j_whole), NG, S]) if j_whole else None
        w2h = sb("w2h", [P, len(j_split), NG, S], F32R) if j_split else None
        w2l = sb("w2l", [P, len(j_split), NG, S], F32R) if j_split else None
        w1 = sb("w1", [P, NF, S])
        w1h = sb("w1h", [P, NF, S], F32R) if f_split else None
        w1l = sb("w1l", [P, NF, S], F32R) if f_split else None
        spread = sb("spread", [P, NSPREAD, P], BF16)
        wt1 = sb("wt1", [P, 3, N1])
        wt2 = sb("wt2", [P, N1 // P, N2])
        wt3 = sb("wt3", [P, N2 // P])
        bias1 = sb("bias1", [P, 1])
        bias2 = sb("bias2", [P, 1])
        biast1 = sb("biast1", [P, N1 // P])
        biast2 = sb("biast2", [P, N2 // P])
        ident = sb("ident", [P, P], BF16)
        ctx_t = sb("ctx_t", [P, P])
        idx = sb("idx", [P, M], I32)
        emb = sb("emb", [P, M * D])
        rest = sb("rest", [P, M * D])
        embp = sb("embp", [P, PARTS, M * D], BF16)
        e_t = sb("e_t", [P, E_RING, CH], BF16)
        a_sb = sb("a_sb", [P, 2, CH])
        zf = sb("zf", [P, F_RING[0], CH])
        zfh = sb("zfh", [P, F_RING[1], CH], F32R) if f_split else None
        zfl = sb("zfl", [P, F_RING[2], CH], F32R) if f_split else None
        zj = sb("zj", [P, J_RING[0], GH, CH])
        zjh = sb("zjh", [P, J_RING[1], GH, CH], F32R) if j_split else None
        zjl = sb("zjl", [P, J_RING[2], GH, CH], F32R) if j_split else None
        x1 = sb("x1", [P, 2, CH])
        x1r = sb("x1r", [P, 2, NG, CH])
        x2 = sb("x2", [P, 1, CH])
        acc1 = sb("acc1", [P, CH])
        acc2 = sb("acc2", [P, CH])
        p1 = sb("p1", [P, P])
        p2 = sb("p2", [P, P])
        h1 = sb("h1", [P, N1 // P, P])
        h2 = sb("h2", [P, N2 // P, P])
        y = sb("y", [P, 1])

        w1_back = x1r[:, 0, :, :].rearrange("p g n -> p (g n)")[:, 0:NF * S]
        spread_f = x1r[:, :, :, :].rearrange("p r g n -> p (r g n)")[0:PARTS * M, NF * S:(NF + NSPREAD) * P]
        ident_f = x1[:, 0, 0:P]
        w2_f = zj[:, :, :, :].rearrange("p r g n -> p (r g n)")[:, 0:len(j_split) * NG * S]

        bank_f = ps("bank_f", [P, 2, CH])
        bank_j = ps("bank_j", [P, 2, CH])
        l1_acc = ps("l1_acc", [P, CH])
        l2_acc = ps("l2_acc", [P, 2, CH])
        misc = ps("misc", [P, CH])
        misc_t = misc[:, :].bitcast(BF16)

        in_w2, in_w1, in_small = sem("in_w2"), sem("in_w1"), sem("in_small")
        in_w2_split, in_spread, in_ident = sem("in_w2_split"), sem("in_spread"), sem("in_ident")
        in_idx, in_ctx, in_emb = sem("in_idx"), sem("in_ctx"), sem("in_emb")
        gather_begun, out_done = sem("gather_begun"), sem("out_done")
        spread_ready, w1_summed = sem("spread_ready"), sem("w1_summed")
        w_rounded, w_ready = sem("w_rounded"), sem("w_ready")
        parts_step, parts_done = sem("parts_step"), sem("parts_done")
        transposed, et_ready = sem("transposed"), sem("et_ready")
        f_spread, j_spread, a_copied = sem("f_spread"), sem("j_spread"), sem("a_copied")
        f_made, j_made = sem("f_made"), sem("j_made")
        f_rounded, j_rounded = sem("f_rounded"), sem("j_rounded")
        f_sub = {BY_DVE: sem("f_sub_dve"), BY_POOL: sem("f_sub_pool")}
        j_sub = {BY_DVE: sem("j_sub_dve"), BY_POOL: sem("j_sub_pool")}
        f_used, j_used = sem("f_used"), sem("j_used")
        x1_done, x2_done, x1_spread = sem("x1_done"), sem("x2_done"), sem("x1_spread")
        acc1_done, acc2_done = sem("acc1_done"), sem("acc2_done")
        p1_done, p2_done = sem("p1_done"), sem("p2_done")
        mlp_mm, mlp_act, y_free = sem("mlp_mm"), sem("mlp_act"), sem("y_free")

        def upto(i, q, per_chunk, t=0):
            return i * (CPT * per_chunk) + (q * per_chunk + t)

        def mlp_upto(tile, layer):
            return (tile + 1) * 3 + layer

        def split_upto(modes, kinds, i, q, t):
            n = len(modes[0])
            row = [m in kinds for r in modes for m in r]
            k = q * n + t
            while k < 0:
                i, k = i - 1, k + CPT * n
            while k > CPT * n:
                i, k = i + 1, k - CPT * n
            return i * sum(row) + sum(row[:k])

        def wait(eng, s, value):
            if isinstance(value, int) and value <= 0:
                return
            eng.wait_ge(s, value)

        class Work:

            def __init__(self, modes, ring, made, rounded, sub, used, z, zh, zl):
                self.ring = ring
                self.modes, self.n = modes, len(modes[0])
                self.made, self.rounded, self.sub, self.used = made, rounded, sub, used
                self.z, self.zh, self.zl = z, zh, zl

            def mode(self, q, t):
                k = (q * self.n + t) % (CPT * self.n)
                return self.modes[k // self.n][k % self.n]

            def slots(self, q, t):
                return [(q * self.n + t) % r for r in self.ring]

            def z_free(self, eng, i, q, t):
                u = t - self.ring[0]
                mode = self.mode(q, u)
                if mode == WHOLE:
                    wait(eng, self.used, upto(i, q, self.n, u + 1))
                else:
                    wait(eng, self.rounded, split_upto(self.modes, (BY_DVE, BY_POOL), i, q, u + 1))
                    wait(eng, self.sub[mode], split_upto(self.modes, (mode,), i, q, u + 1))

            def part_free(self, eng, part, i, q, t):
                wait(eng, self.used, upto(i, q, self.n, t - self.ring[part] + 1))

        F = Work(F_MODE, F_RING, f_made, f_rounded, f_sub, f_used, zf, zfh, zfl)
        J = Work(J_MODE, J_RING, j_made, j_rounded, j_sub, j_used, zj, zjh, zjl)

        def item(i, q, c, k):
            kind, t, ahead = SEQ[k % NS]
            ahead += k // NS
            if c is not None and not 0 <= c + ahead < CHUNKS:
                return None
            return kind, t, i, q + ahead

        LOOP_TILES = TILES - 2

        def run(eng, step):
            for c in range(-2, 2):
                step(0, c, c)
            with eng.Fori(0, LOOP_TILES) as i:
                for q in range(2, CPT + 2):
                    step(i, q, None)
            for c in range(CPT * LOOP_TILES + 2, CHUNKS + 1):
                step(c // CPT, c % CPT, c)

        def norm(i, q):
            return i + q // CPT, q % CPT

        block = ctx.enter_context(nc.Block())

        @block.sync
        def _(sp):
            sp.sem_inc(mlp_mm, 3)
            sp.sem_inc(mlp_act, 3)
            sp.sem_inc(y_free, 1)
            sp.dma_start(idx[:, :], dram["ids"][0:P, :]).then_inc(in_idx, 16)
            sp.dma_start(spread_f, dram["spread"]).then_inc(in_spread, 16)
            sp.dma_start(ident_f, dram["ident"]).then_inc(in_ident, 16)
            sp.dma_start(w1[:, :, :], dram["w1_ahead"]).then_inc(in_w1, 16)
            sp.dma_start(w1_back, dram["w1_back"].rearrange("p t s -> p (t s)")).then_inc(in_w1, 16)
            for k, j in enumerate(j_split):
                sp.dma_start(w2_f[:, k * NG * S:(k + 1) * NG * S],
                             dram["w2"][:, j].rearrange("p g s -> p (g s)")).then_inc(in_w2_split, 16)
            for k, j in enumerate(j_whole):
                sp.dma_start(w2[:, k], dram["w2"][:, j]).then_inc(in_w2, 16)
            sp.dma_start(wt1[:, 0:2, :], dram["W_top1"][0:2 * S, :].rearrange("(k p) n -> p k n", p=P)
                         ).then_inc(in_small, 16)
            sp.dma_start(wt1[0:NCTX, 2, :], dram["W_top1"][2 * S:, :]).then_inc(in_small, 16)
            sp.dma_start(wt2[:, :, :], dram["W_top2"].rearrange("(k p) n -> p k n", p=P)).then_inc(in_small, 16)
            for dst, name in ((wt3, "W_top3"), (bias1, "b1"), (bias2, "b2"), (biast1, "b_top1"),
                              (biast2, "b_top2")):
                sp.dma_start(dst[:, :], dram[name]).then_inc(in_small, 16)

            def step(i, q, c):
                tile, cq = norm(i, q)
                if cq == 2 and (c is None or tile + 2 < TILES):
                    rows = bass.ds((tile + 2) * P, P)
                    wait(sp, in_emb, (tile + 2) * (16 * M))
                    sp.dma_start(idx[:, :], dram["ids"][rows, :]).then_inc(in_idx, 16)
                if cq == 0 and (c is None or c > 0):
                    store(tile - 1)
                for k in range(NS):
                    it = item(i, q, c, k - X_LAG)
                    if it and it[0] == "X1":
                        spread_x1(it[2], it[3])

            def spread_x1(i, q):
                s = q % 2
                wait(sp, x1_done, upto(i, q, 1, 1))
                for r in range(ML):
                    for g in range(NG):
                        sp.dma_start(x1r[HL * r:HL * (r + 1), s, g, :], x1[HL * g:HL * (g + 1), s, :]
                                     ).then_inc(x1_spread, 16)

            def store(tile):
                row = tile * P
                sp.wait_ge(mlp_mm, mlp_upto(tile, 0))
                sp.dma_start(ctx_t[0:NCTX, :], dram["ctx_t"][:, bass.ds(row, P)]).then_inc(in_ctx, 16)
                sp.wait_ge(mlp_act, mlp_upto(tile, 3))
                sp.dma_start(out[bass.ds(row, P), :], y[:, :]).then_inc(out_done, 16)
                sp.wait_ge(out_done, (tile + 1) * 16)
                sp.sem_inc(y_free, 1)

            run(sp, step)
            sp.wait_ge(out_done, 16 * TILES)

        @block.gpsimd
        def _(pool):
            def gather(tile, fields):
                for f in fields:
                    if f == 0:
                        wait(pool, parts_done, tile)
                        pool.wait_ge(in_idx, (tile + 1) * 16)
                        pool.sem_inc(gather_begun, 1)
                    nc.gpsimd.indirect_dma_start(
                        out=emb[:, f * D:(f + 1) * D], out_offset=None, in_=tables[f],
                        in_offset=bass.IndirectOffsetOnAxis(ap=idx[:, f:f + 1], axis=0),
                    ).then_inc(in_emb, 16)

            def subtract(w, t, i, q):
                if w.mode(q, t) != BY_POOL:
                    return
                w.part_free(pool, 2, i, q, t)
                pool.wait_ge(w.rounded, split_upto(w.modes, (BY_DVE, BY_POOL), i, q, t + 1))
                zs, hs, ls = w.slots(q, t)
                nc.gpsimd.tensor_tensor(w.zl[:, ls], w.z[:, zs], w.zh[:, hs].bitcast(F32),
                                        ALU.subtract).then_inc(w.sub[BY_POOL], 1)

            def step(i, q, c):
                tile, cq = norm(i, q)
                tile += 2 if cq >= 2 else 1
                fields = list(GATHER_SHARE[cq]) if c is None or tile < TILES else []
                for k in range(NS):
                    if fields and k in GATHER_AT:
                        gather(tile, [fields.pop(0)])
                    it = item(i, q, c, k - SUB_LAG)
                    if it and it[0] in "FJ":
                        subtract(F if it[0] == "F" else J, it[1], it[2], it[3])

            gather(0, range(M))
            run(pool, step)

        @block.scalar
        def _(act):
            act.wait_ge(in_ident, 16)
            nc.scalar.copy(ident[:, :], ident_f).then_inc(spread_ready, 1)
            act.wait_ge(in_spread, 16)
            nc.scalar.copy(spread[0:PARTS * M, :, :].rearrange("p u n -> p (u n)"), spread_f
                           ).then_inc(spread_ready, 1)
            if f_split:
                act.wait_ge(w1_summed, 1)
                nc.scalar.copy(w1h[:, :, :], w1[:, :, :]).then_inc(w_rounded, 1)
            if j_split:
                act.wait_ge(in_w2_split, 16 * len(j_split))
                nc.scalar.copy(w2h[:, :, :, :].rearrange("p j g s -> p (j g s)"), w2_f).then_inc(w_rounded, 1)
            act.wait_ge(in_small, 16 * 8)

            def copy_transposed(i, q):
                act.wait_ge(transposed, upto(i, q, 1, 1))
                wait(act, j_spread, upto(i, q - E_RING + 1, NJ))
                nc.scalar.copy(e_t[0:PARTS * M, q % E_RING, :], misc_t[0:PARTS * M, 0:CH]).then_inc(et_ready, 1)

            def copy_a(i, q):
                act.wait_ge(f_spread, upto(i, q, 1 + NF, 1))
                wait(act, f_made, upto(i, q - 1, NF))
                nc.scalar.copy(a_sb[:, q % 2, :], bank_f[:, 0, :]).then_inc(a_copied, 1)

            def round_z(w, t, i, q):
                if w.mode(q, t) == WHOLE:
                    return
                w.part_free(act, 1, i, q, t)
                act.wait_ge(w.made, upto(i, q, w.n, t + 1))
                zs, hs, _ = w.slots(q, t)
                nc.scalar.copy(w.zh[:, hs], w.z[:, zs]).then_inc(w.rounded, 1)

            def end_layer1(i, q):
                act.wait_ge(f_used, upto(i, q, NF, NF))
                wait(act, x1_spread, upto(i, q - 1, 16 * ML * NG))
                wait(act, acc1_done, upto(i, q - 1, 1))
                wait(act, j_made, upto(i, q - 1, NU))
                nc.scalar.activation(x1[:, q % 2, :], l1_acc[:, :], ACT.Relu, bias=bias1[:, 0:1]
                                     ).then_inc(x1_done, 1)

            def end_layer2(i, q):
                act.wait_ge(j_used, upto(i, q, NU, NU))
                wait(act, acc2_done, upto(i, q, 1))
                nc.scalar.activation(x2[:, 0, :], l2_acc[:, q % 2, :], ACT.Relu, bias=bias2[:, 0:1]
                                     ).then_inc(x2_done, 1)

            def mlp(tile, layer):
                act.wait_ge(mlp_mm, mlp_upto(tile, layer))
                if layer == 3:
                    act.wait_ge(y_free, tile + 1)
                    nc.scalar.copy(y[:, :], misc[:, 0:1]).then_inc(mlp_act, 1)
                    return
                dst, bias, n = ((h1, biast1, N1), (h2, biast2, N2))[layer - 1]
                for k in range(n // P):
                    last = nc.scalar.activation(dst[:, k, :], misc[:, k * P:(k + 1) * P], ACT.Relu,
                                                bias=bias[:, k:k + 1])
                last.then_inc(mlp_act, 1)

            def step(i, q, c):
                tile, cq = norm(i, q)
                for k in range(NS):
                    it = item(i, q, c, k)
                    if it and it[0] == "T":
                        copy_transposed(it[2], it[3])
                    if it and it[0] == "A":
                        copy_a(it[2], it[3])
                    if it and it[0] in "FJ":
                        round_z(F if it[0] == "F" else J, it[1], it[2], it[3])
                    it = item(i, q, c, k - X_LAG)
                    if it and it[0] == "X1":
                        end_layer1(it[2], it[3])
                    if it and it[0] == "X2":
                        end_layer2(it[2], it[3])
                    if cq == 0 and (c is None or c > 0) and k - X_LAG in MLP_AT:
                        mlp(tile - 1, MLP_AT[k - X_LAG])

            run(act, step)

        @block.vector
        def _(dve):
            dve.wait_ge(in_w1, 32)
            nc.vector.tensor_tensor(w1[:, :, :].rearrange("p t s -> p (t s)"),
                                    w1[:, :, :].rearrange("p t s -> p (t s)"), w1_back,
                                    ALU.add).then_inc(w1_summed, 1)
            if f_split:
                dve.wait_ge(w1_summed, 1)
                dve.wait_ge(w_rounded, 1)
                nc.vector.tensor_tensor(w1l[:, :, :], w1[:, :, :], w1h[:, :, :].bitcast(F32),
                                        ALU.subtract).then_inc(w_ready, 1)
            if j_split:
                dve.wait_ge(w_rounded, 1 + f_split)
                nc.vector.tensor_tensor(w2l[:, :, :, :].rearrange("p j g s -> p (j g s)"), w2_f,
                                        w2h[:, :, :, :].bitcast(F32).rearrange("p j g s -> p (j g s)"),
                                        ALU.subtract).then_inc(w_ready, 1)
            if j_split:
                dve.wait_ge(w_ready, 1 + f_split)

            def make_parts(tile):
                dve.wait_ge(in_emb, (tile + 1) * (16 * M))
                wait(dve, transposed, tile * CPT)
                nc.vector.tensor_copy(embp[:, 0, :], emb[:, :]).then_inc(parts_step, 1)
                dve.wait_ge(parts_step, tile * 3 + 1)
                nc.vector.tensor_tensor(rest[:, :], emb[:, :], embp[:, 0, :], ALU.subtract
                                        ).then_inc(parts_step, 1)
                dve.wait_ge(parts_step, tile * 3 + 2)
                nc.vector.tensor_copy(embp[:, 1, :], rest[:, :]).then_inc(parts_step, 1)
                dve.wait_ge(parts_step, tile * 3 + 3)
                nc.vector.tensor_tensor(embp[:, 2, :], rest[:, :], embp[:, 1, :], ALU.subtract
                                        ).then_inc(parts_done, 1)

            def make_f(t, i, q):
                dve.wait_ge(f_spread, upto(i, q, 1 + NF, t + 2))
                if t == 0:
                    dve.wait_ge(a_copied, upto(i, q, 1, 1))
                F.z_free(dve, i, q, t)
                nc.vector.tensor_tensor(zf[:, F.slots(q, t)[0], :], a_sb[:, q % 2, :],
                                        bank_f[:, (t + 1) % 2, :], ALU.mult).then_inc(f_made, 1)

            def make_j(t, i, q):
                j, half = divmod(t, NH)
                dve.wait_ge(j_spread, upto(i, q, NJ, j + 1))
                if t == 0:
                    dve.wait_ge(x1_spread, upto(i, q, 16 * ML * NG, 16 * ML * NG))
                J.z_free(dve, i, q, t)
                e_row = bank_j[:, j % 2:j % 2 + 1, :].broadcast_to([P, GH, CH])
                nc.vector.tensor_tensor(zj[:, J.slots(q, t)[0]], x1r[:, q % 2, GH * half:GH * (half + 1)],
                                        e_row, ALU.mult).then_inc(j_made, 1)

            def subtract(w, t, i, q):
                if w.mode(q, t) != BY_DVE:
                    return
                w.part_free(dve, 2, i, q, t)
                dve.wait_ge(w.rounded, split_upto(w.modes, (BY_DVE, BY_POOL), i, q, t + 1))
                zs, hs, ls = w.slots(q, t)
                nc.vector.tensor_tensor(w.zl[:, ls], w.z[:, zs], w.zh[:, hs].bitcast(F32),
                                        ALU.subtract).then_inc(w.sub[BY_DVE], 1)

            def sum_d(i, q, x, x_done, acc, acc_done, p, p_done):
                tile, cq = norm(i, q)
                dve.wait_ge(x_done, upto(i, q, 1, 1))
                if cq == 0:
                    wait(dve, p_done, tile)
                    nc.vector.tensor_copy(acc[:, :], x[:, q % x.shape[1], :]).then_inc(acc_done, 1)
                    return
                dve.wait_ge(acc_done, upto(i, q, 1))
                nc.vector.tensor_tensor(acc[:, :], acc[:, :], x[:, q % x.shape[1], :], ALU.add).then_inc(acc_done, 1)
                if cq == CPT - 1:
                    dve.wait_ge(acc_done, upto(i, q, 1, 1))
                    dve.wait_ge(mlp_mm, mlp_upto(tile, 0))
                    nc.vector.tensor_reduce(p[:, :], acc[:, :].rearrange("p (d b) -> p b d", d=DC),
                                            AX.X, ALU.add).then_inc(p_done, 1)

            def step(i, q, c):
                tile, cq = norm(i, q)
                if c == -2:
                    make_parts(0)
                for k in range(NS):
                    it = item(i, q, c, k)
                    if it and it[0] == "F":
                        make_f(it[1], it[2], it[3])
                    if it and it[0] == "J":
                        make_j(it[1], it[2], it[3])
                    it = item(i, q, c, k - SUB_LAG)
                    if it and it[0] in "FJ":
                        subtract(F if it[0] == "F" else J, it[1], it[2], it[3])
                    it = item(i, q, c, k - ACC_LAG)
                    if it and it[0] == "X1":
                        sum_d(it[2], it[3], x1, x1_done, acc1, acc1_done, p1, p1_done)
                    if it and it[0] == "X2":
                        sum_d(it[2], it[3], x2, x2_done, acc2, acc2_done, p2, p2_done)
                    if k == PARTS_AT and cq == 2 and c != -2 and (c is None or tile + 1 < TILES):
                        make_parts(tile + 1)

            run(dve, step)

        @block.tensor
        def _(pe):
            pe.wait_ge(spread_ready, 2)
            pe.wait_ge(w1_summed, 1)
            wait(pe, in_w2, 16 * len(j_whole))
            wait(pe, w_ready, f_split + bool(j_split))
            pe.wait_ge(in_small, 16 * 8)
            emb_by_d = embp[:, :, :].rearrange("p a (f d) -> p d (a f)", d=D)

            def transpose_chunk(i, q, c):
                tile, cq = norm(i, q)
                pe.wait_ge(parts_done, tile + 1)
                wait(pe, et_ready, upto(i, q, 1))
                if c is None or c > 0:
                    pe.wait_ge(mlp_act, mlp_upto(tile - (1 if cq < 2 else 0), 0))
                for d in range(DC):
                    last = nc.tensor.transpose(misc_t[0:PARTS * M, d * P:(d + 1) * P],
                                               emb_by_d[:, cq * DC + d, :], ident[:, :])
                last.then_inc(transposed, 1)

            def spread_f_rows(u, i, q):
                if u == 0:
                    pe.wait_ge(et_ready, upto(i, q, 1, 1))
                if u == 2:
                    pe.wait_ge(a_copied, upto(i, q, 1, 1))
                else:
                    wait(pe, f_made, upto(i, q, NF, u - 2 if u > 2 else u - 1))
                nc.tensor.matmul(bank_f[:, u % 2, :], spread[0:PARTS * M, u, :],
                                 e_t[0:PARTS * M, q % E_RING, :], start=True, stop=True).then_inc(f_spread, 1)

            def spread_j_rows(t, i, q):
                wait(pe, j_made, upto(i, q, NU, NH * (t - 1)))
                nc.tensor.matmul(bank_j[:, t % 2, :], spread[0:PARTS * M, 1 + NF + t, :],
                                 e_t[0:PARTS * M, q % E_RING, :], start=True, stop=True).then_inc(j_spread, 1)

            def contract(w, t, i, q, acc, rows, tiles):
                mode = w.mode(q, t)
                if mode == WHOLE:
                    pe.wait_ge(w.made, upto(i, q, w.n, t + 1))
                    passes = [(0, 3)]
                else:
                    pe.wait_ge(w.rounded, split_upto(w.modes, (BY_DVE, BY_POOL), i, q, t + 1))
                    passes = [(1, 4), (2, 4), (1, 5)]
                for k, (a, b) in enumerate(passes):
                    if b == 5:
                        pe.wait_ge(w.sub[mode], split_upto(w.modes, (mode,), i, q, t + 1))
                    for g, ops in enumerate(tiles):
                        last = nc.tensor.matmul(acc, ops[a][0:rows], ops[b][0:rows],
                                                start=(t == 0 and k == 0 and g == 0),
                                                stop=(t == w.n - 1 and k == len(passes) - 1
                                                      and g == len(tiles) - 1))
                last.then_inc(w.used, 1)

            def contract_f(t, i, q):
                if t == 0:
                    wait(pe, x1_done, upto(i, q, 1))
                zs, hs, ls = F.slots(q, t)
                split = F.mode(q, t) != WHOLE
                contract(F, t, i, q, l1_acc[:, :], F_ROWS[t],
                         [(w1[:, t, :], split and w1h[:, t, :], split and w1l[:, t, :],
                           zf[:, zs, :], split and zfh[:, hs, :], split and zfl[:, ls, :])])

            def contract_j(t, i, q):
                if t == 0:
                    wait(pe, x2_done, upto(i, q - 1, 1))
                zs, hs, ls = J.slots(q, t)
                split = J.mode(q, t) != WHOLE
                j, half = divmod(t, NH)
                kw, ks = None if split else j_whole.index(j), j_split.index(j) if split else None
                contract(J, t, i, q, l2_acc[:, q % 2, :], J_ROWS[j],
                         [(split or w2[:, kw, g, :], split and w2h[:, ks, g, :], split and w2l[:, ks, g, :],
                           zj[:, zs, g % GH, :], split and zjh[:, hs, g % GH, :],
                           split and zjl[:, ls, g % GH, :])
                          for g in range(GH * half, GH * (half + 1))])

            def mlp(tile, layer):
                if layer == 1:
                    pe.wait_ge(p1_done, tile + 1)
                    pe.wait_ge(p2_done, tile + 1)
                    pe.wait_ge(in_ctx, (tile + 1) * 16)
                    if isinstance(tile, int) and tile == TILES - 1:
                        pe.wait_ge(et_ready, CHUNKS)
                    else:
                        pe.wait_ge(et_ready, upto(tile + 1, 1, 1, 1))
                    src = [(p1[:, :], wt1[:, 0, :]), (p2[:, :], wt1[:, 1, :]),
                           (ctx_t[0:NCTX, :], wt1[0:NCTX, 2, :])]
                    n = N1
                elif layer == 2:
                    pe.wait_ge(mlp_act, mlp_upto(tile, 1))
                    src = [(h1[:, k, :], wt2[:, k, :]) for k in range(N1 // P)]
                    n = N2
                else:
                    pe.wait_ge(mlp_act, mlp_upto(tile, 2))
                    for k in range(N2 // P):
                        last = nc.tensor.matmul(misc[:, 0:1], h2[:, k, :], wt3[:, k:k + 1],
                                                start=(k == 0), stop=(k == N2 // P - 1))
                    last.then_inc(mlp_mm, 1)
                    return
                for o in range(n // P):
                    for k, (x, w) in enumerate(src):
                        last = nc.tensor.matmul(misc[:, o * P:(o + 1) * P], w[:, o * P:(o + 1) * P], x,
                                                start=(k == 0), stop=(k == len(src) - 1))
                last.then_inc(mlp_mm, 1)

            def spread_item(it, c):
                if it is None:
                    return
                if it[0] == "T":
                    transpose_chunk(it[2], it[3], c)
                if it[0] == "A":
                    spread_f_rows(0, it[2], it[3])
                if it[0] == "F":
                    spread_f_rows(it[1] + 1, it[2], it[3])
                if it[0] == "J" and it[1] % NH == 0:
                    spread_j_rows(it[1] // NH, it[2], it[3])

            def step(i, q, c):
                tile, cq = norm(i, q)
                if c == -2:
                    for k in range(SPREAD_AHEAD):
                        spread_item(item(i, q, c, k), c)
                for k in range(NS):
                    it = item(i, q, c, k)
                    spread_item(item(i, q, c, k + SPREAD_AHEAD), c)
                    if it and it[0] == "F":
                        contract_f(it[1], it[2], it[3])
                    if it and it[0] == "J":
                        contract_j(it[1], it[2], it[3])
                    if cq == 0 and (c is None or c > 0) and k in MLP_AT:
                        mlp(tile - 1, MLP_AT[k])

            run(pe, step)


def kernel(**inputs):
    from concourse import bacc
    from concourse.bass_utils import run_bass_kernel_spmd

    nc = bacc.Bacc("TRN2", target_bir_lowering=False, num_devices=1)
    arrays = {}

    def load(name, a):
        a = np.ascontiguousarray(a)
        arrays[name] = a
        return nc.dram_tensor(name, a.shape, mybir.dt.from_np(a.dtype), kind="ExternalInput").ap()

    def columns(a):
        return np.asarray(a).reshape(-1, P).T

    ahead, back = pair_weights(inputs["L0_rec_W1"])
    dram = {
        "ids": load("ids", inputs["ids"]),
        "spread": load("spread_const", spread_matrices().reshape(PARTS * M, NSPREAD * P)),
        "ident": load("ident_const", np.eye(P, dtype=np.float32)),
        "w1_ahead": load("w1_ahead", ahead),
        "w1_back": load("w1_back", back),
        "w2": load("w2_pairs", cross_weights(inputs["L0_rec_W2"])),
        "ctx_t": load("ctx_transposed", np.asarray(inputs["dense_ctx"]).T),
        "W_top1": load("w_top1", inputs["W_top1"]),
        "W_top2": load("w_top2", inputs["W_top2"]),
        "W_top3": load("w_top3", columns(inputs["W_top3"])),
        "b1": load("cin_b1", columns(inputs["L0_rec_b1"])),
        "b2": load("cin_b2", columns(inputs["L0_rec_b2"])),
        "b_top1": load("mlp_b1", columns(inputs["b_top1"])),
        "b_top2": load("mlp_b2", columns(inputs["b_top2"])),
    }
    tables = [load(f"tbl_{f}", inputs[f"tbl_{f}"]) for f in range(M)]
    out = nc.dram_tensor("y_out", (B, 1), F32, kind="ExternalOutput").ap()
    build(nc, dram, tables, out)
    result = run_bass_kernel_spmd(nc, [arrays], core_ids=[0])
    return result.results[0]["y_out"]
```
